# Optimizing a Trainium2 kernel written in Bass

```python
import numpy as np
import jax
import jax.numpy as jnp

def _softmax(x, axis=-1):
    return jax.nn.softmax(x, axis=axis)

def _gelu(x):
    return jax.nn.gelu(x, approximate=True)

def _silu(x):
    return jax.nn.silu(x)

def _sigmoid(x):
    return jax.nn.sigmoid(x)

def _layernorm(x, axis=-1, eps=1e-05):
    m = jnp.mean(x, axis=axis, keepdims=True)
    v = jnp.var(x, axis=axis, keepdims=True)
    return (x - m) / jnp.sqrt(v + eps)

def _scatter_add(tgt, idx, src, axis=0):
    return tgt.at[idx].add(src)

def _segment_sum(src, seg, n):
    return jax.ops.segment_sum(src, seg, n)
kernel_name = 'mk_gnn_resnorm_d1_gnn_r8_e7dcf2'

def setup_inputs(seed: int=0):
    np.random.seed(seed)
    _w = jnp.asarray

    def _rec_inputs():
        import jax
        import jax.numpy as jnp
        _gk = jax.random.key(seed)
        x = -0.0008691 + 1 * jax.random.normal(jax.random.fold_in(_gk, 1), (12500, 128), jnp.float32)
        src = jax.random.randint(jax.random.fold_in(_gk, 2), (400000,), 0, 12500, jnp.int32)
        dst = jax.random.randint(jax.random.fold_in(_gk, 3), (400000,), 0, 12500, jnp.int32)
        _o = jnp.argsort(dst, stable=True)
        src = src[_o]
        dst = dst[_o]
        edge_type_2 = jax.random.randint(jax.random.fold_in(_gk, 12), (400000,), 0, 2, jnp.int32)
        return (x, src, dst, edge_type_2)
    x, src, dst, edge_type_2 = _rec_inputs()

    def _L0_gnn_setup():
        import jax, jax.numpy as jnp
        import numpy as np
        IN_DIM = 128
        OUT_DIM = 128
        N_NODES = 1250
        N_EDGES = 80000
        key = jax.random.key(seed)
        ks = jax.random.split(key, 9)
        X = jax.random.normal(ks[0], (N_NODES, IN_DIM), dtype=jnp.float32)
        edge_index = jax.random.randint(ks[1], (2, N_EDGES), 0, N_NODES, dtype=jnp.int64)
        edge_types = jax.random.randint(ks[2], (N_EDGES,), 0, 2, dtype=jnp.int64)
        s = 1.0 / np.sqrt(IN_DIM)
        W_data = jax.random.uniform(ks[3], (OUT_DIM, IN_DIM), minval=-s, maxval=s, dtype=jnp.float32)
        b_data = jax.random.uniform(ks[4], (OUT_DIM,), minval=-s, maxval=s, dtype=jnp.float32)
        W_control = jax.random.uniform(ks[5], (OUT_DIM, IN_DIM), minval=-s, maxval=s, dtype=jnp.float32)
        b_control = jax.random.uniform(ks[6], (OUT_DIM,), minval=-s, maxval=s, dtype=jnp.float32)
        W_self = jax.random.uniform(ks[7], (OUT_DIM, IN_DIM), minval=-s, maxval=s, dtype=jnp.float32)
        b_self = jax.random.uniform(ks[8], (OUT_DIM,), minval=-s, maxval=s, dtype=jnp.float32)
        return {'X': X, 'edge_index': edge_index, 'edge_types': edge_types, 'W_data': W_data, 'b_data': b_data, 'W_control': W_control, 'b_control': b_control, 'W_self': W_self, 'b_self': b_self}
    _L0_gnn_all = _L0_gnn_setup()
    _L0_gnn_in = {k: v for k, v in _L0_gnn_all.items() if k in ('W_data', 'b_data', 'W_control', 'b_control', 'W_self', 'b_self')}
    del _L0_gnn_all
    return {'x': x, 'src': src, 'dst': dst, 'edge_type_2': edge_type_2, 'L0_gnn_W_data': _L0_gnn_in['W_data'], 'L0_gnn_b_data': _L0_gnn_in['b_data'], 'L0_gnn_W_control': _L0_gnn_in['W_control'], 'L0_gnn_b_control': _L0_gnn_in['b_control'], 'L0_gnn_W_self': _L0_gnn_in['W_self'], 'L0_gnn_b_self': _L0_gnn_in['b_self']}

def reference(x, src, dst, edge_type_2, L0_gnn_W_data, L0_gnn_b_data, L0_gnn_W_control, L0_gnn_b_control, L0_gnn_W_self, L0_gnn_b_self):
    import jax
    import jax.numpy as jnp

    def _L0_gnn_ref(X, edge_index, edge_types, W_data, b_data, W_control, b_control, W_self, b_self):
        import jax, jax.numpy as jnp
        import numpy as np
        IN_DIM = 128
        OUT_DIM = 128
        N_NODES = 1250
        N_EDGES = 80000
        src, dst = (edge_index[0], edge_index[1])
        Xs = X[src]
        m_data = Xs @ W_data.T + b_data
        m_ctrl = Xs @ W_control.T + b_control
        msg = jnp.where((edge_types == 0)[:, None], m_data, m_ctrl)
        agg = jax.ops.segment_sum(msg, dst, num_segments=X.shape[0])
        out = agg + (X @ W_self.T + b_self)
        return jax.nn.relu(out)
    edge_index = jnp.stack([src, dst])
    x = _layernorm(x + _L0_gnn_ref(x, edge_index, edge_type_2, L0_gnn_W_data, L0_gnn_b_data, L0_gnn_W_control, L0_gnn_b_control, L0_gnn_W_self, L0_gnn_b_self), axis=-1)
    return x

_drawn_inputs = setup_inputs


def setup_inputs(seed=0):
    import zlib

    import numpy as np

    out = dict(_drawn_inputs(seed))
    spreads = {}
    factors = {'L0_gnn_b_self': 3.344}
    for name, (base, spread) in spreads.items():
        noise = np.random.default_rng([zlib.crc32(name.encode()), seed]).standard_normal(out[name].shape)
        drawn = base * np.exp(spread * noise) if base else spread * noise
        out[name] = jnp.asarray(drawn.astype(out[name].dtype))
    for name, factor in factors.items():
        out[name] = (out[name] * factor).astype(out[name].dtype)
    return out
```

```python
from contextlib import ExitStack

import numpy as np

import concourse.bass as bass
from concourse import mybir

F32 = mybir.dt.float32
I32 = mybir.dt.int32
ALU = mybir.AluOpType
ACT = mybir.ActivationFunctionType
AX = mybir.AxisListType

P = 128
GT = 5
WIN = 64
RING = 25
GPI = RING // GT
CH = 125
SB = 4
WIDE = SB * P
XS = 4
EPS = 1e-5


def gnn_resnorm(nc, x, src, dst, etype, w_data, b_data, w_ctrl, b_ctrl, w_self, b_self, out):
    N, D = x.shape
    E, = src.shape
    assert D == P and E % (P * CH) == 0 and CH % RING == 0 and RING % GT == 0
    TILES = E // P
    GROUPS = TILES // GT
    ITERS = TILES // RING
    CHUNKS = TILES // CH
    CG = CH // GT
    FULL_SUPER = N // WIDE
    TAIL = N - FULL_SUPER * WIDE
    TAIL_ROWS = [min(P, TAIL - j * P) for j in range(-(-TAIL // P))]
    SUPERS = FULL_SUPER + 1
    assert TAIL and FULL_SUPER > XS and ITERS > 2 and CHUNKS >= 2
    NPAD = -(-(N + WIN) // WIDE) * WIDE
    WINDOWS = NPAD // WIDE

    table = nc.dram_tensor("message_table", (2 * N, D), F32, kind="Internal").ap()
    table_of = table.rearrange("(n t) d -> n (t d)", t=2)

    ctx = ExitStack()
    with ctx:
        def sb(name, shape, dt=F32):
            return ctx.enter_context(nc.sbuf_tensor(name, shape, dt))

        def ps(name, shape):
            return ctx.enter_context(nc.psum_tensor(name, shape, F32))

        def sem(name):
            return ctx.enter_context(nc.semaphore(name))

        x_sb = sb("x_sb", [P, SUPERS * SB, D])
        acc = sb("acc", [P, NPAD])
        idx_all = sb("idx_all", [P, TILES])
        rel_all = sb("rel_all", [P, TILES])
        idx_now = sb("idx_now", [P, RING], I32)
        rows = sb("rows", [P, RING, D])
        hot = sb("hot", [P, GPI, GT, WIN])
        bases = sb("bases", [1, GROUPS], I32)
        ident = sb("ident", [P, P])
        w_nat = sb("w_nat", [P, 3, D])
        w_t = sb("w_t", [P, 3, D])
        b_row = sb("b_row", [P, 2 * D])
        b_col = sb("b_col", [P, 1])
        x_t = sb("x_t", [P, 2, WIDE])
        y_sb = sb("y_sb", [P, 2, SB, 2 * D])
        src_n = sb("src_n", [CH, 2, P], I32)
        typ_n = sb("typ_n", [CH, 2, P], I32)
        dst_n = sb("dst_n", [CH, 2, P], I32)
        base_n = sb("base_n", [CH, CHUNKS], I32)
        base_f = sb("base_f", [CH, CHUNKS])
        idx_n = sb("idx_n", [CH, 2, P])
        rel_n = sb("rel_n", [CH, 2, P])
        iota_i = sb("iota_i", [P, WIDE], I32)
        iota_w = sb("iota_w", [P, WIDE])
        eps_t = sb("eps_t", [P, 1])
        ext = sb("ext", [P, 4])
        viol = sb("viol", [1, 2])
        flag = sb("flag", [1, 1], I32)
        late_i = sb("late_i", [P, 1], I32)
        late = sb("late", [P, 6])
        late_key = sb("late_key", [P, 1])
        late_hot = sb("late_hot", [P, WIDE])
        late_row = sb("late_row", [P, D])
        late_idx = sb("late_idx", [P, 1], I32)
        stats = sb("stats", [P, 2, SB, 6])
        mv = sb("mv", [P, 2, SB, 2])
        rstd = sb("rstd", [P, 2, SB])
        std = sb("std", [P, 2, SB])
        shift = sb("shift", [P, 2, SB])
        out_sb = sb("out_sb", [P, 2, SB, D])

        bank = [ps(f"bank{i}", [P, WIDE]) for i in range(8)]
        window_ps = bank[0:GPI]
        iota_ps = bank[GPI]
        late_ps = bank[6]

        consts_loaded = sem("consts_loaded")
        bases_loaded = sem("bases_loaded")
        x_loaded = [sem(f"x_loaded{i}") for i in range(XS)]
        edges_loaded = [sem(f"edges_loaded{i}") for i in range(2)]
        pool_consts = sem("pool_consts")
        ident_ready = sem("ident_ready")
        iota_ready = sem("iota_ready")
        weights_ready = sem("weights_ready")
        w_transposed = sem("w_transposed")
        x_transposed = sem("x_transposed")
        xt_ready = sem("xt_ready")
        self_done = sem("self_done")
        acc_seeded = sem("acc_seeded")
        msg_done = sem("msg_done")
        msg_ready = sem("msg_ready")
        table_written = [sem(f"table_written{i}") for i in range(2)]
        chunk_ready = sem("chunk_ready")
        chunk_transposed = sem("chunk_transposed")
        chunk_stored = sem("chunk_stored")
        staged = sem("staged")
        gather_turn = sem("gather_turn")
        gathered = [sem(f"gathered{i}") for i in range(RING)]
        hot_ready = sem("hot_ready")
        group_done = sem("group_done")
        group_added = sem("group_added")
        vchain = sem("vchain")
        late_chain = sem("late_chain")
        ext_ready = sem("ext_ready")
        ext_transposed = sem("ext_transposed")
        flag_ready = sem("flag_ready")
        late_loaded = sem("late_loaded")
        late_gathered = sem("late_gathered")
        late_hot_ready = sem("late_hot_ready")
        late_matmul = sem("late_matmul")
        late_added = sem("late_added")
        late_tile_done = sem("late_tile_done")
        acc_complete = sem("acc_complete")
        block_back = sem("block_back")
        res_ready = sem("res_ready")
        mv_ready = sem("mv_ready")
        std_ready = sem("std_ready")
        norm_ready = sem("norm_ready")
        out_ready = sem("out_ready")
        out_written = [sem(f"out_written{i}") for i in range(2)]

        block = ctx.enter_context(nc.Block())

        src_v = src.rearrange("(t e) -> t e", e=P)
        typ_v = etype.rearrange("(t e) -> t e", e=P)
        dst_v = dst.rearrange("(t e) -> t e", e=P)
        dst_groups = dst.rearrange("(g e) -> g e", e=GT * P)
        dst_cg = dst.rearrange("(c g e) -> g c e", g=CG, e=GT * P)

        def rows_of(s):
            return [P] * SB if s is None else TAIL_ROWS

        @block.sync
        def _(sp):
            for k, w in enumerate((w_self, w_data, w_ctrl)):
                sp.dma_start(w_nat[:, k, :], w).then_inc(consts_loaded, 16)
            for k, b in enumerate((b_data, b_ctrl)):
                sp.dma_start(b_row[:, k * D:(k + 1) * D], b.partition_broadcast(P)).then_inc(consts_loaded, 16)
            sp.dma_start(b_col[:, :], b_self.rearrange("(d o) -> d o", o=1)).then_inc(consts_loaded, 16)

            def load_x(s, slot):
                sp.dma_start(x_sb[:, bass.ds(s * SB, SB), :],
                             x[bass.ds(s * WIDE, WIDE), :].rearrange("(j p) d -> p j d", p=P)
                             ).then_inc(x_loaded[slot], 16)

            for s in range(XS):
                load_x(s, s)
            for s in range(XS, FULL_SUPER):
                sp.wait_ge(x_transposed, s - XS + 1)
                load_x(s, s % XS)
            sp.wait_ge(x_transposed, FULL_SUPER - XS + 1)
            for j, r in enumerate(TAIL_ROWS):
                n0 = FULL_SUPER * WIDE + j * P
                sp.dma_start(x_sb[0:r, FULL_SUPER * SB + j, :], x[n0:n0 + r, :]
                             ).then_inc(x_loaded[FULL_SUPER % XS], 16)

            sp.wait_ge(flag_ready, 1)
            outside = sp.value_load(flag[0:1, 0:1], min_val=0, max_val=1)
            with sp.If(outside > 0):
                with sp.Fori(0, TILES) as t:
                    sp.wait_ge(late_tile_done, t + 1)
                    sp.dma_start(late_i[:, :], dst_v[bass.ds(t, 1), :].rearrange("o e -> e o"),
                                 allow_slow_non_contiguous=True).then_inc(late_loaded, 16)

            def store_out(s, slot, count):
                sp.wait_ge(out_ready, count)
                sp.dma_start(out[bass.ds(s * WIDE, WIDE), :].rearrange("(j p) d -> p j d", p=P),
                             out_sb[:, slot, :, :]).then_inc(out_written[slot], 16)

            for s in range(FULL_SUPER):
                store_out(s, s % 2, s + 1)
            sp.wait_ge(out_ready, FULL_SUPER + 1)
            for j, r in enumerate(TAIL_ROWS):
                n0 = FULL_SUPER * WIDE + j * P
                sp.dma_start(out[n0:n0 + r, :], out_sb[0:r, FULL_SUPER % 2, j, :]
                             ).then_inc(out_written[FULL_SUPER % 2], 16)
            n_even = (FULL_SUPER + 1) // 2
            n_odd = FULL_SUPER // 2
            tail_dmas = len(TAIL_ROWS)
            for slot, n in ((0, n_even), (1, n_odd)):
                n += tail_dmas if FULL_SUPER % 2 == slot else 0
                sp.wait_ge(out_written[slot], 16 * n)

        @block.gpsimd
        def _(pool):
            pool.memset(ident[:, :], 0.0).then_inc(pool_consts, 1)
            pool.iota(iota_i[:, :], pattern=[[1, WIDE]], base=0, channel_multiplier=0).then_inc(iota_ready, 1)
            pool.wait_ge(pool_consts, 1)
            pool.affine_select(out=ident[:, :], in_=ident[:, :], compare_op=ALU.not_equal, fill=1.0, base=0,
                               pattern=[[-1, P]], channel_multiplier=1).then_inc(ident_ready, 1)
            pool.dma_start(bases[:, :], dst_groups[:, 0:1].rearrange("g o -> o g"),
                           allow_slow_non_contiguous=True).then_inc(bases_loaded, 16)

            for r in range(GT):
                pool.dma_start(base_n[r::GT, :], dst_cg[:, :, 0], allow_slow_non_contiguous=True
                               ).then_inc(bases_loaded, 16)

            pool.wait_ge(table_written[0], 16 * ((FULL_SUPER + 1) // 2)
                         + (16 * len(TAIL_ROWS) if FULL_SUPER % 2 == 0 else 0))
            pool.wait_ge(table_written[1], 16 * (FULL_SUPER // 2)
                         + (16 * len(TAIL_ROWS) if FULL_SUPER % 2 == 1 else 0))

            def gather_iteration(it):
                for q in range(GPI):
                    pool.wait_ge(staged, it * GPI + q + 1)
                    pool.sem_inc(gather_turn, 1)
                    for j in range(GT):
                        slot = q * GT + j
                        pool.indirect_dma_start(
                            out=rows[:, slot, :], out_offset=None, in_=table,
                            in_offset=bass.IndirectOffsetOnAxis(ap=idx_now[:, slot:slot + 1], axis=0),
                        ).then_inc(gathered[slot], 16)

            with pool.Fori(0, ITERS) as it:
                gather_iteration(it)

            pool.wait_ge(flag_ready, 1)
            outside = pool.value_load(flag[0:1, 0:1], min_val=0, max_val=1)
            with pool.If(outside > 0):
                with pool.Fori(0, TILES) as t:
                    pool.wait_ge(late_hot_ready, t * (WINDOWS + 1) + 1)
                    pool.sem_inc(gather_turn, 1)
                    pool.indirect_dma_start(
                        out=late_row[:, :], out_offset=None, in_=table,
                        in_offset=bass.IndirectOffsetOnAxis(ap=late_idx[:, 0:1], axis=0),
                    ).then_inc(late_gathered, 16)

        @block.tensor
        def _(pe):
            pe.wait_ge(ident_ready, 1)
            pe.wait_ge(consts_loaded, 16 * 6)
            for k in range(3):
                last = pe.transpose(bank[7][:, k * D:(k + 1) * D], w_nat[:, k, :], ident[:, :])
            last.then_inc(weights_ready, 1)
            pe.wait_ge(w_transposed, 1)

            def transpose_x(s, slot, rows_in, loaded, count):
                pe.wait_ge(x_loaded[slot % XS], loaded)
                if count >= 2:
                    pe.wait_ge(xt_ready, count - 1)
                for j, r in enumerate(rows_in):
                    last = pe.transpose(bank[count % 2][:, j * P:j * P + r], x_sb[0:r, s * SB + j, :],
                                        ident[0:r, 0:r])
                last.then_inc(x_transposed, 1)

            def multiply_x(s, rows_in):
                n = sum(rows_in)
                pe.wait_ge(xt_ready, s + 1)
                if s >= 1:
                    pe.wait_ge(acc_seeded, s)
                pe.matmul(bank[6][:, 0:n], w_t[:, 0, :], x_t[:, s % 2, 0:n], start=True, stop=True
                          ).then_inc(self_done, 1)
                if s >= 1:
                    pe.wait_ge(msg_ready, s)
                for j, r in enumerate(rows_in):
                    last = pe.matmul(bank[2 + j][0:r, 0:2 * D], x_t[:, s % 2, j * P:j * P + r],
                                     w_t[:, 1:3, :].rearrange("p k d -> p (k d)"), start=True, stop=True)
                last.then_inc(msg_done, 1)

            def loaded_by(s):
                return 16 * (s // XS + 1) if s < FULL_SUPER else 16 * (s // XS + len(TAIL_ROWS))

            transpose_x(0, 0, [P] * SB, loaded_by(0), 0)
            for s in range(SUPERS):
                if s + 1 < SUPERS:
                    transpose_x(s + 1, s + 1, [P] * SB if s + 1 < FULL_SUPER else TAIL_ROWS,
                                loaded_by(s + 1), s + 1)
                multiply_x(s, [P] * SB if s < FULL_SUPER else TAIL_ROWS)

            pe.wait_ge(acc_seeded, SUPERS)
            pe.wait_ge(msg_ready, SUPERS)
            for c in range(CHUNKS):
                pe.wait_ge(chunk_ready, c + 1)
                if c >= 2:
                    pe.wait_ge(chunk_stored, c - 1)
                pe.transpose(bank[6 + c % 2][:, 0:CH], idx_n[:, c % 2, :], ident[0:CH, 0:CH])
                pe.transpose(bank[6 + c % 2][:, P:P + CH], rel_n[:, c % 2, :], ident[0:CH, 0:CH]
                             ).then_inc(chunk_transposed, 1)

            pe.wait_ge(ext_ready, 1)
            pe.transpose(bank[6][0:1, 0:P], ext[:, 2:3], ident[:, :]).then_inc(ext_transposed, 1)

            def scatter_iteration(it, first):
                for q in range(GPI):
                    pe.wait_ge(hot_ready, it * GPI + q + 1)
                    if not first:
                        pe.wait_ge(group_added, (it - 1) * GPI + q + 1)
                    for j in range(GT):
                        slot = q * GT + j
                        pe.wait_ge(gathered[slot], (it + 1) * 16)
                        last = pe.matmul(window_ps[q][:, 0:WIN], rows[:, slot, :], hot[:, q, j, :],
                                         start=(j == 0), stop=(j == GT - 1))
                    last.then_inc(group_done, 1)

            scatter_iteration(0, True)
            with pe.Fori(1, ITERS) as it:
                scatter_iteration(it, False)

            pe.wait_ge(flag_ready, 1)
            outside = pe.value_load(flag[0:1, 0:1], min_val=0, max_val=1)
            with pe.If(outside > 0):
                with pe.Fori(0, TILES) as t:
                    with pe.Fori(0, WINDOWS) as w:
                        pe.wait_ge(late_gathered, (t + 1) * 16)
                        pe.wait_ge(late_hot_ready, t * (WINDOWS + 1) + w + 2)
                        pe.matmul(late_ps[:, :], late_row[:, :], late_hot[:, :], start=True, stop=True
                                  ).then_inc(late_matmul, 1)

            pe.wait_ge(acc_complete, 1)
            for s in range(SUPERS):
                if s >= 2:
                    pe.wait_ge(res_ready, s - 1)
                for j, r in enumerate([P] * SB if s < FULL_SUPER else TAIL_ROWS):
                    n0 = s * WIDE + j * P
                    last = pe.transpose(bank[s % 2][0:r, j * P:(j + 1) * P], acc[:, n0:n0 + r], ident[:, :])
                last.then_inc(block_back, 1)

        @block.scalar
        def _(act):
            def load_chunk(c):
                t0 = c * CH
                for buf, view in ((src_n, src_v), (typ_n, typ_v), (dst_n, dst_v)):
                    act.dma_start(buf[:, c % 2, :], view[t0:t0 + CH, :]).then_inc(edges_loaded[c % 2], 16)

            load_chunk(0)
            load_chunk(1)

            act.wait_ge(weights_ready, 1)
            act.activation(w_t[:, :, :].rearrange("p k d -> p (k d)"), bank[7][:, 0:3 * D], ACT.Copy
                           ).then_inc(w_transposed, 1)

            for s in range(SUPERS):
                n = WIDE if s < FULL_SUPER else TAIL
                act.wait_ge(x_transposed, s + 1)
                if s >= 2:
                    act.wait_ge(msg_done, s - 1)
                act.activation(x_t[:, s % 2, 0:n], bank[s % 2][:, 0:n], ACT.Copy).then_inc(xt_ready, 1)
                act.wait_ge(self_done, s + 1)
                act.activation(acc[:, s * WIDE:s * WIDE + n], bank[6][:, 0:n], ACT.Identity, bias=b_col[:, 0:1]
                               ).then_inc(acc_seeded, 1)
                act.wait_ge(msg_ready, s + 1)
                if s < FULL_SUPER:
                    act.dma_start(table_of[s * WIDE:(s + 1) * WIDE, :].rearrange("(j p) d -> p j d", p=P),
                                  y_sb[:, s % 2, :, :]).then_inc(table_written[s % 2], 16)
                else:
                    for j, r in enumerate(TAIL_ROWS):
                        n0 = s * WIDE + j * P
                        act.dma_start(table_of[n0:n0 + r, :], y_sb[0:r, s % 2, j, :]
                                      ).then_inc(table_written[s % 2], 16)

            for c in range(2, CHUNKS):
                act.wait_ge(chunk_ready, c - 1)
                load_chunk(c)

            def stage_iteration(it, first):
                for q in range(GPI):
                    if not first:
                        act.wait_ge(group_done, (it - 1) * GPI + q + 1)
                    act.activation(idx_now[:, q * GT:(q + 1) * GT],
                                   idx_all[:, bass.ds(it * RING + q * GT, GT)], ACT.Copy).then_inc(staged, 1)

            for it in range(CH // RING):
                if it == 0:
                    act.wait_ge(chunk_stored, 1)
                stage_iteration(it, it == 0)
            act.wait_ge(chunk_stored, CHUNKS)
            with act.Fori(CH // RING, ITERS) as it:
                stage_iteration(it, False)

            for s in range(SUPERS):
                rows_in = [P] * SB if s < FULL_SUPER else TAIL_ROWS
                act.wait_ge(mv_ready, s + 1)
                act.activation(std[:, s % 2, 0:len(rows_in)], mv[:, s % 2, 0:len(rows_in), 1], ACT.Sqrt,
                               bias=eps_t[:, 0:1]).then_inc(std_ready, 1)
                act.wait_ge(norm_ready, s + 1)
                if s >= 2:
                    n_before = (s - 2) // 2 + 1
                    act.wait_ge(out_written[s % 2], 16 * n_before)
                for j, r in enumerate(rows_in):
                    last = act.activation(out_sb[0:r, s % 2, j, :], x_sb[0:r, s * SB + j, :], ACT.Identity,
                                          bias=shift[0:r, s % 2, j:j + 1], scale=rstd[0:r, s % 2, j:j + 1])
                last.then_inc(out_ready, 1)

        @block.vector
        def _(dve):
            links = [0]

            def link(ins):
                links[0] += 1
                ins.then_inc(vchain, 1)
                dve.wait_ge(vchain, links[0])

            dve.memset(eps_t[:, :], EPS)
            dve.memset(acc[:, N:NPAD], 0.0)
            dve.memset(mv[:, :, :, :], 1.0)
            dve.wait_ge(iota_ready, 1)
            link(dve.tensor_copy(iota_w[:, :], iota_i[:, :]))

            dve.wait_ge(consts_loaded, 16 * 6)
            for s in range(SUPERS):
                dve.wait_ge(msg_done, s + 1)
                if s >= 2:
                    dve.wait_ge(table_written[s % 2], 16 * ((s - 2) // 2 + 1))
                for j, r in enumerate([P] * SB if s < FULL_SUPER else TAIL_ROWS):
                    last = dve.tensor_tensor(y_sb[0:r, s % 2, j, :], bank[2 + j][0:r, 0:2 * D], b_row[0:r, :],
                                             ALU.add)
                last.then_inc(msg_ready, 1)

            dve.wait_ge(bases_loaded, 16 * (1 + GT))
            link(dve.tensor_copy(base_f[:, :], base_n[:, :]))

            def store_chunk(c):
                dve.wait_ge(chunk_transposed, c + 1)
                dve.tensor_copy(idx_all[:, c * CH:(c + 1) * CH], bank[6 + c % 2][:, 0:CH])
                dve.tensor_copy(rel_all[:, c * CH:(c + 1) * CH], bank[6 + c % 2][:, P:P + CH]
                                ).then_inc(chunk_stored, 1)

            for c in range(CHUNKS):
                dve.wait_ge(edges_loaded[c % 2], 48 * (c // 2 + 1))
                if c >= 2:
                    dve.wait_ge(chunk_transposed, c - 1)
                dve.scalar_tensor_tensor(out=idx_n[:, c % 2, :], in0=src_n[:, c % 2, :], scalar=2.0,
                                         in1=typ_n[:, c % 2, :], op0=ALU.mult, op1=ALU.add)
                dve.tensor_scalar(rel_n[:, c % 2, :], dst_n[:, c % 2, :], base_f[:, c:c + 1], None,
                                  ALU.subtract).then_inc(chunk_ready, 1)
                if c >= 1:
                    store_chunk(c - 1)
            store_chunk(CHUNKS - 1)

            dve.wait_ge(chunk_stored, CHUNKS)
            dve.tensor_reduce(ext[:, 0:1], rel_all[:, :], AX.X, ALU.max)
            link(dve.tensor_reduce(ext[:, 1:2], rel_all[:, :], AX.X, ALU.min, negate=True))
            dve.scalar_tensor_tensor(out=ext[:, 2:3], in0=ext[:, 0:1], scalar=float(1 - WIN), in1=ext[:, 1:2],
                                     op0=ALU.add, op1=ALU.max).then_inc(ext_ready, 1)
            dve.wait_ge(ext_transposed, 1)
            link(dve.tensor_reduce(viol[0:1, 0:1], bank[6][0:1, 0:P], AX.X, ALU.max))
            dve.tensor_single_scalar(flag[0:1, 0:1], viol[0:1, 0:1], 0.0, ALU.is_gt).then_inc(flag_ready, 1)

            link(dve.tensor_copy(iota_ps[:, 0:WIN], iota_w[:, 0:WIN]))

            def make_hot(g, q, wait_for):
                if wait_for is not None:
                    dve.wait_ge(group_done, wait_for)
                dve.tensor_tensor(hot[:, q, :, :],
                                  iota_ps[:, 0:WIN].unsqueeze(1).to_broadcast([P, GT, WIN]),
                                  rel_all[:, bass.ds(g * GT, GT)].unsqueeze(2).to_broadcast([P, GT, WIN]),
                                  ALU.is_equal).then_inc(hot_ready, 1)

            def add_group(g, q, first):
                base = dve.value_load(bases[0:1, bass.ds(g, 1)], min_val=0, max_val=N - 1)
                dve.wait_ge(group_done, g + 1)
                if not first:
                    dve.wait_ge(group_added, g)
                dve.tensor_tensor(acc[:, bass.ds(base, WIN)], window_ps[q][:, 0:WIN],
                                  acc[:, bass.ds(base, WIN)], ALU.add).then_inc(group_added, 1)

            def iteration(it, first, last):
                for q in range(GPI):
                    if not (last and q == GPI - 1):
                        nq = (q + 1) % GPI
                        free = None if first and q + 1 < GPI else it * GPI + q + 1 + 1 - GPI
                        make_hot(it * GPI + q + 1, nq, free)
                    add_group(it * GPI + q, q, first and q == 0)

            dve.wait_ge(acc_seeded, SUPERS)
            make_hot(0, 0, None)
            iteration(0, True, False)
            with dve.Fori(1, ITERS - 1) as it:
                iteration(it, False, False)
            iteration(ITERS - 1, False, True)

            outside = dve.value_load(flag[0:1, 0:1], min_val=0, max_val=1)
            dve.wait_ge(group_added, GROUPS)
            dve.sem_inc(late_tile_done, 1)
            with dve.If(outside > 0):
                LINKS = 4 + WINDOWS
                with dve.Fori(0, TILES) as t:
                    rel = rel_all[:, bass.ds(t, 1)]
                    dve.wait_ge(late_loaded, (t + 1) * 16)
                    dve.tensor_single_scalar(late[:, 0:1], rel, 0.0, ALU.is_ge)
                    dve.tensor_single_scalar(late[:, 1:2], rel, float(WIN), ALU.is_lt)
                    dve.tensor_single_scalar(late[:, 2:3], late_i[:, :], 1.0, ALU.add).then_inc(late_chain, 1)
                    dve.wait_ge(late_chain, t * LINKS + 1)
                    dve.tensor_tensor(late[:, 3:4], late[:, 0:1], late[:, 1:2], ALU.mult).then_inc(late_chain, 1)
                    dve.wait_ge(late_chain, t * LINKS + 2)
                    dve.tensor_scalar(late[:, 4:5], late[:, 3:4], -1.0, 1.0, ALU.mult, ALU.add
                                      ).then_inc(late_chain, 1)
                    dve.wait_ge(late_chain, t * LINKS + 3)
                    dve.scalar_tensor_tensor(out=late[:, 5:6], in0=late[:, 4:5], scalar=1.0, in1=late[:, 2:3],
                                             op0=ALU.mult, op1=ALU.mult).then_inc(late_chain, 1)
                    dve.wait_ge(late_chain, t * LINKS + 4)
                    dve.tensor_single_scalar(late_key[:, :], late[:, 5:6], -1.0, ALU.add)
                    dve.tensor_copy(late_idx[:, :], idx_all[:, bass.ds(t, 1)]).then_inc(late_hot_ready, 1)
                    with dve.Fori(0, WINDOWS) as w:
                        dve.wait_ge(late_hot_ready, t * (WINDOWS + 1) + w + 1)
                        dve.tensor_scalar(late_hot[:, :], iota_w[:, :], late_key[:, 0:1], None, ALU.is_equal
                                          ).then_inc(late_hot_ready, 1)
                        dve.wait_ge(late_hot_ready, t * (WINDOWS + 1) + w + 2)
                        dve.tensor_single_scalar(late_key[:, :], late_key[:, :], float(-WIDE), ALU.add
                                                 ).then_inc(late_chain, 1)
                        dve.wait_ge(late_matmul, t * WINDOWS + w + 1)
                        dve.tensor_tensor(acc[:, bass.ds(w * WIDE, WIDE)], late_ps[:, :],
                                          acc[:, bass.ds(w * WIDE, WIDE)], ALU.add).then_inc(late_added, 1)
                        dve.wait_ge(late_added, t * WINDOWS + w + 1)
                        dve.wait_ge(late_chain, t * LINKS + w + 5)
                    dve.sem_inc(late_tile_done, 1)
            dve.sem_inc(acc_complete, 1)

            for s in range(SUPERS):
                rows_in = [P] * SB if s < FULL_SUPER else TAIL_ROWS
                k, h = len(rows_in), s % 2
                dve.wait_ge(block_back, s + 1)
                if s >= 2:
                    dve.wait_ge(out_ready, s - 1)
                for j, r in enumerate(rows_in):
                    last = dve.scalar_tensor_tensor(out=x_sb[0:r, s * SB + j, :],
                                                    in0=bank[h][0:r, j * P:(j + 1) * P], scalar=0.0,
                                                    in1=x_sb[0:r, s * SB + j, :], op0=ALU.max, op1=ALU.add)
                last.then_inc(res_ready, 1)
                dve.wait_ge(res_ready, s + 1)
                for j, r in enumerate(rows_in):
                    last = dve.bn_stats(stats[0:r, h, j, :], x_sb[0:r, s * SB + j, :])
                link(last)
                for j, r in enumerate(rows_in):
                    last = dve.bn_aggr(mv[0:r, h, j, :], stats[0:r, h, j, :])
                last.then_inc(mv_ready, 1)
                dve.wait_ge(mv_ready, s + 1)
                dve.wait_ge(std_ready, s + 1)
                link(dve.reciprocal(rstd[:, h, 0:k], std[:, h, 0:k]))
                dve.scalar_tensor_tensor(out=shift[:, h, 0:k], in0=mv[:, h, 0:k, 0], scalar=-1.0,
                                         in1=rstd[:, h, 0:k], op0=ALU.mult, op1=ALU.mult
                                         ).then_inc(norm_ready, 1)


_INS = ["x", "src", "dst", "edge_type_2", "L0_gnn_W_data", "L0_gnn_b_data", "L0_gnn_W_control",
        "L0_gnn_b_control", "L0_gnn_W_self", "L0_gnn_b_self"]


def kernel(**inputs):
    import concourse.bacc as bacc
    from concourse.bass_utils import run_bass_kernel_spmd

    nc = bacc.Bacc("TRN2", target_bir_lowering=False, num_devices=1)
    arrays, args = {}, []
    for name in _INS:
        a = np.ascontiguousarray(inputs[name])
        arrays[f"in_{name}"] = a
        args.append(nc.dram_tensor(f"in_{name}", a.shape, mybir.dt.from_np(a.dtype), kind="ExternalInput").ap())
    out = nc.dram_tensor("out", arrays["in_x"].shape, F32, kind="ExternalOutput").ap()
    gnn_resnorm(nc, *args, out)
    r = run_bass_kernel_spmd(nc, [arrays], core_ids=[0])
    return r.results[0]["out"]
```

```python
from contextlib import ExitStack

import numpy as np

import concourse.bass as bass
from concourse import mybir

F32 = mybir.dt.float32
I32 = mybir.dt.int32
ALU = mybir.AluOpType
ACT = mybir.ActivationFunctionType
AX = mybir.AxisListType

P = 128
GT = 5
WIN = 32
RING = 25
GPI = RING // GT
CH = 125
IPC = CH // RING
GPC = CH // GT
SB = 4
WIDE = SB * P
LAG = 2
TYPE_STEP = 16384
EPS = 1e-5


def gnn_resnorm(nc, x, src, dst, etype, w_data, b_data, w_ctrl, b_ctrl, w_self, b_self, out):
    N, D = x.shape
    E, = src.shape
    TILES = E // P
    GROUPS = TILES // GT
    ITERS = TILES // RING
    CHUNKS = TILES // CH
    FULL_SUPER = N // WIDE
    TAIL = N - FULL_SUPER * WIDE
    TAIL_ROWS = [min(P, TAIL - j * P) for j in range(-(-TAIL // P))]
    SUPERS = FULL_SUPER + 1
    NPAD = -(-(N + WIN) // WIDE) * WIDE
    WINDOWS = NPAD // WIDE
    PARTS = len(TAIL_ROWS)
    assert D == P and E % (P * CH) == 0 and CH % RING == 0 and RING % GT == 0 and N < TYPE_STEP - WIN
    assert TAIL and SB % PARTS == 0 and SUPERS == CHUNKS and CHUNKS % 2 == 1 and CHUNKS >= 7

    ctx = ExitStack()
    with ctx:
        def sb(name, shape, dt=F32):
            return ctx.enter_context(nc.sbuf_tensor(name, shape, dt))

        def sem(name):
            return ctx.enter_context(nc.semaphore(name))

        x_in = sb("x_in", [P, 2, SB, D])
        x_res = sb("x_res", [P, SB, D])
        acc_now = sb("acc_now", [P, WIDE])
        acc = sb("acc", [P, NPAD])
        src_all = sb("src_all", [P, TILES + RING])
        key_all = sb("key_all", [P, TILES + GT])
        src_now = sb("src_now", [P, RING], I32)
        rows = sb("rows", [P, RING, D])
        hot = sb("hot", [P, GPI, GT, 2, WIN])
        hot_sum = sb("hot_sum", [P, GPI, 2, WIN])
        sums = sb("sums", [P, GPI, 2, WIN])
        bases = sb("bases", [1, GROUPS], I32)
        ident = sb("ident", [P, P])
        w_nat = sb("w_nat", [P, 3, D])
        w_t = sb("w_t", [P, 3, D])
        b_row = sb("b_row", [P, 2 * D])
        b_col = sb("b_col", [P, 1])
        late_typ = sb("late_typ", [P, 1], I32)
        x_t = sb("x_t", [P, WIDE])
        src_n = sb("src_n", [CH, 2, P], I32)
        typ_n = sb("typ_n", [CH, 2, P], I32)
        dst_n = sb("dst_n", [CH, 2, P], I32)
        base_n = sb("base_n", [CH, CHUNKS], I32)
        base_f = sb("base_f", [CH, CHUNKS])
        src_f = sb("src_f", [CH, 2, P])
        rel_f = sb("rel_f", [CH, 2, P])
        key_f = sb("key_f", [CH, 2, P])
        rel_max = sb("rel_max", [CH, CHUNKS])
        rel_min = sb("rel_min", [CH, CHUNKS])
        floor_i = sb("floor_i", [CH, CHUNKS], I32)
        out_of = sb("out_of", [CH, 4, CHUNKS])
        worst = sb("worst", [P, 1])
        viol = sb("viol", [1, 1])
        flag = sb("flag", [1, 1], I32)
        iota_i = sb("iota_i", [P, WIDE], I32)
        hot_i = sb("hot_i", [P, 2, WIN], I32)
        eps_t = sb("eps_t", [P, 1])
        y_sb = sb("y_sb", [P, SB, D])
        stats = sb("stats", [P, SB, 6])
        mv = sb("mv", [P, SB, 2])
        std = sb("std", [P, SB])
        rstd = sb("rstd", [P, SB])
        shift = sb("shift", [P, SB])
        out_sb = sb("out_sb", [P, SB, D])
        iota_w = sb("iota_w", [P, WIDE])
        late_dst = sb("late_dst", [P, 1], I32)
        late_src = sb("late_src", [P, 1], I32)
        late = sb("late", [P, 8])
        late_key = sb("late_key", [P, 1])
        late_x = sb("late_x", [P, D])
        late_xt = sb("late_xt", [P, D])
        late_both = sb("late_both", [P, 2 * D])
        minus_one = sb("minus_one", [P, 1])
        late_part = sb("late_part", [P, D])
        late_msg = sb("late_msg", [P, D])
        late_hot = sb("late_hot", [P, WIDE])

        bank = [ctx.enter_context(nc.psum_tensor(f"bank{i}", [P, WIDE], F32)) for i in range(8)]
        group_ps = bank[0:GPI]
        SUMS = slice(0, 2 * WIN)
        MSGS = slice(2 * WIN, 3 * WIN)
        hot_ps = bank[GPI]
        turn_ps = bank[6]
        node_ps = bank[7]

        weights_loaded = sem("weights_loaded")
        bases_loaded = sem("bases_loaded")
        x_loaded = [sem(f"x_loaded{i}") for i in range(2)]
        sources_loaded = [sem(f"sources_loaded{i}") for i in range(2)]
        edges_loaded = [sem(f"edges_loaded{i}") for i in range(2)]
        res_loaded = sem("res_loaded")
        super_copied = sem("super_copied")
        ident_zero = sem("ident_zero")
        ident_ready = sem("ident_ready")
        iota_ready = sem("iota_ready")
        pads_ready = sem("pads_ready")
        weights_turned = sem("weights_turned")
        wt_ready = sem("wt_ready")
        rel_ready = sem("rel_ready")
        start_step = sem("start_step")
        worst_step = sem("worst_step")
        sources_ready = sem("sources_ready")
        sources_turned = sem("sources_turned")
        sources_stored = sem("sources_stored")
        lists_ready = sem("lists_ready")
        lists_turned = sem("lists_turned")
        lists_stored = sem("lists_stored")
        x_turned = sem("x_turned")
        xt_ready = sem("xt_ready")
        self_ready = sem("self_ready")
        self_added = sem("self_added")
        staged = sem("staged")
        gather_turn = sem("gather_turn")
        gathered = [sem(f"gathered{i}") for i in range(RING)]
        hot_ready = sem("hot_ready")
        hot_summed = sem("hot_summed")
        rows_used = sem("rows_used")
        sums_ready = sem("sums_ready")
        msgs_ready = sem("msgs_ready")
        window_added = sem("window_added")
        super_turned = sem("super_turned")
        y_ready = sem("y_ready")
        dve_turn = sem("dve_turn")
        dve_step = sem("dve_step")
        mv_ready = sem("mv_ready")
        std_ready = sem("std_ready")
        scales_ready = sem("scales_ready")
        out_ready = sem("out_ready")
        out_written = sem("out_written")
        out_free = sem("out_free")
        worst_ready = sem("worst_ready")
        worst_turned = sem("worst_turned")
        flag_ready = sem("flag_ready")
        late_loaded = sem("late_loaded")
        late_index = sem("late_index")
        late_gathered = sem("late_gathered")
        late_turned = sem("late_turned")
        late_xt_ready = sem("late_xt_ready")
        late_both_ready = sem("late_both_ready")
        late_step = sem("late_step")
        late_msg_step = sem("late_msg_step")
        late_hot_ready = sem("late_hot_ready")
        late_summed = sem("late_summed")
        late_added = sem("late_added")
        late_tile_done = sem("late_tile_done")

        block = ctx.enter_context(nc.Block())

        src_v = src.rearrange("(t e) -> t e", e=P)
        typ_v = etype.rearrange("(t e) -> t e", e=P)
        dst_v = dst.rearrange("(t e) -> t e", e=P)
        dst_groups = dst.rearrange("(g e) -> g e", e=GT * P)
        dst_cg = dst.rearrange("(c g e) -> g c e", g=GPC, e=GT * P)

        def rows_in(tail):
            return TAIL_ROWS if tail else [P] * SB

        def over_chunks(eng, body):
            body(0, 0, False)
            body(1, 1, False)
            with eng.Fori(0, (CHUNKS - 3) // 2) as i:
                body(2 * i + 2, 0, False)
                body(2 * i + 3, 1, False)
            body(CHUNKS - 1, 0, True)

        def after_loop(body):
            for s in range(CHUNKS - LAG, SUPERS):
                body(s, s, s == FULL_SUPER)

        def again(eng, body):
            with eng.Fori(0, FULL_SUPER) as s:
                body(s, s + SUPERS, False)
            body(FULL_SUPER, FULL_SUPER + SUPERS, True)

        def early(c):
            return isinstance(c, int) and c < LAG

        def chunk_pair(c, h):
            return c // 2 + 1 if isinstance(c, int) else (c - h + 2) // 2

        @block.sync
        def _(sp):
            def load_lists(c, h):
                for buf, view, loaded in ((src_n, src_v, sources_loaded[h]), (dst_n, dst_v, edges_loaded[h]),
                                          (typ_n, typ_v, edges_loaded[h])):
                    sp.dma_start(buf[:, h, :], view[bass.ds(c * CH, CH), :]).then_inc(loaded, 16)

            def move(s, tail, sbuf, dram, to_sbuf, moved):
                for j in range(PARTS):
                    if tail:
                        r, n0 = TAIL_ROWS[j], s * WIDE + j * P
                        a, b = sbuf[0:r, j, :], dram[n0:n0 + r, :]
                    else:
                        k = SB // PARTS
                        a = sbuf[:, j * k:(j + 1) * k, :]
                        b = dram[bass.ds(s * WIDE + j * k * P, k * P), :].rearrange("(k p) d -> p k d", p=P)
                    sp.dma_start(*((a, b) if to_sbuf else (b, a))).then_inc(moved, 16)

            def load_x(s, h, tail):
                move(s, tail, x_in[:, h, :, :], x, True, x_loaded[h])

            load_lists(0, 0)
            for r in range(GT):
                sp.dma_start(base_n[r::GT, :], dst_cg[:, :, 0], allow_slow_non_contiguous=True
                             ).then_inc(bases_loaded, 16)
            sp.dma_start(bases[:, 0:GROUPS], dst_groups[:, 0:1].rearrange("g o -> o g"),
                         allow_slow_non_contiguous=True).then_inc(bases_loaded, 16)
            for k, w in enumerate((w_self, w_data, w_ctrl)):
                sp.dma_start(w_nat[:, k, :], w).then_inc(weights_loaded, 16)
            for k, b in enumerate((b_data, b_ctrl)):
                sp.dma_start(b_row[:, k * D:(k + 1) * D], b.partition_broadcast(P)).then_inc(weights_loaded, 16)
            sp.dma_start(b_col[:, :], b_self.rearrange("(d o) -> d o", o=1)).then_inc(weights_loaded, 16)
            load_lists(1, 1)
            load_x(0, 0, False)
            load_x(1, 1, False)

            def load_res(s, tail):
                move(s, tail, x_res, x, True, res_loaded)

            def finish(s, count, res_next):
                if res_next is not None:
                    sp.wait_ge(y_ready, count + 2)
                    load_res(s + 1, res_next)
                sp.wait_ge(out_ready, count + 2)
                move(s, res_next is None, out_sb, out, False, out_written)
                sp.wait_ge(out_written, (count + 1) * 16 * PARTS)
                sp.sem_inc(out_free, 1)

            load_res(0, False)
            sp.sem_inc(out_free, 1)

            def chunk(c, h, tail_next):
                sp.wait_ge(lists_turned, c + 1)
                sp.wait_ge(x_turned, c + 1)
                load_lists(c + 2, h)
                load_x(c + 2, h, tail_next)
                if not early(c):
                    finish(c - LAG, c - LAG, False)

            chunk(0, 0, False)
            chunk(1, 1, False)
            with sp.Fori(0, (CHUNKS - 5) // 2) as i:
                chunk(2 * i + 2, 0, False)
                chunk(2 * i + 3, 1, False)
            chunk(CHUNKS - 3, 0, True)
            for c in (CHUNKS - 2, CHUNKS - 1):
                finish(c - LAG, c - LAG, False)
            after_loop(lambda s, count, tail: finish(s, count, None if tail else s + 1 == FULL_SUPER))

            sp.wait_ge(flag_ready, 1)
            general = sp.value_load(flag[0:1, 0:1], min_val=0, max_val=1)
            with sp.If(general > 0):
                with sp.Fori(0, TILES) as t:
                    sp.wait_ge(late_tile_done, t + 1)
                    for buf, view in ((late_dst, dst_v), (late_typ, typ_v)):
                        sp.dma_start(buf[:, :], view[bass.ds(t, 1), :].rearrange("o e -> e o"),
                                     allow_slow_non_contiguous=True).then_inc(late_loaded, 16)
                load_res(0, False)
                with sp.Fori(0, FULL_SUPER - 1) as s:
                    finish(s, s + SUPERS, False)
                finish(FULL_SUPER - 1, FULL_SUPER - 1 + SUPERS, True)
                finish(FULL_SUPER, FULL_SUPER + SUPERS, None)

        @block.gpsimd
        def _(pool):
            pool.memset(ident[:, :], 0.0).then_inc(ident_zero, 1)
            pool.iota(hot_i[:, :, :], pattern=[[TYPE_STEP, 2], [1, WIN]], base=0, channel_multiplier=0
                      ).then_inc(iota_ready, 1)
            pool.wait_ge(ident_zero, 1)
            pool.affine_select(out=ident[:, :], in_=ident[:, :], compare_op=ALU.not_equal, fill=1.0, base=0,
                               pattern=[[-1, P]], channel_multiplier=1).then_inc(ident_ready, 1)
            pool.iota(iota_i[:, :], pattern=[[1, WIDE]], base=0, channel_multiplier=0).then_inc(iota_ready, 1)
            pool.iota(floor_i[:, :], pattern=[[WIDE, CHUNKS]], base=(1 - LAG) * WIDE, channel_multiplier=0
                      ).then_inc(iota_ready, 1)

            with pool.Fori(0, ITERS) as it:
                for q in range(GPI):
                    pool.wait_ge(staged, it * GPI + q + 1)
                    pool.sem_inc(gather_turn, 1)
                    for j in range(GT):
                        slot = q * GT + j
                        pool.indirect_dma_start(
                            out=rows[:, slot, :], out_offset=None, in_=x,
                            in_offset=bass.IndirectOffsetOnAxis(ap=src_now[:, slot:slot + 1], axis=0),
                        ).then_inc(gathered[slot], 16)

            pool.wait_ge(flag_ready, 1)
            general = pool.value_load(flag[0:1, 0:1], min_val=0, max_val=1)
            with pool.If(general > 0):
                with pool.Fori(0, TILES) as t:
                    pool.wait_ge(late_index, t + 1)
                    pool.sem_inc(gather_turn, 1)
                    pool.indirect_dma_start(
                        out=late_x[:, :], out_offset=None, in_=x,
                        in_offset=bass.IndirectOffsetOnAxis(ap=late_src[:, 0:1], axis=0),
                    ).then_inc(late_gathered, 16)

        @block.tensor
        def _(pe):
            pe.sem_inc(rows_used, GPI)
            pe.sem_inc(msgs_ready, GPI)
            pe.sem_inc(super_turned, 1)

            def turn_lists(c, h):
                pe.wait_ge(sources_ready, c + 1)
                pe.transpose(turn_ps[:, 0:CH], src_f[:, h, :], ident[0:CH, 0:CH]).then_inc(sources_turned, 1)
                pe.wait_ge(lists_ready, c + 1)
                pe.wait_ge(sources_stored, c + 1)
                pe.transpose(turn_ps[:, P:P + CH], key_f[:, h, :], ident[0:CH, 0:CH]).then_inc(lists_turned, 1)

            pe.wait_ge(ident_ready, 1)
            turn_lists(0, 0)
            pe.wait_ge(weights_loaded, 16 * 6)
            for k in range(3):
                last = pe.transpose(node_ps[:, k * D:(k + 1) * D], w_nat[:, k, :], ident[:, :])
            last.then_inc(weights_turned, 1)

            def turn_super(count, rows_of):
                pe.wait_ge(super_copied, count + 1)
                for j, r in enumerate(rows_of):
                    last = pe.transpose(node_ps[0:r, j * P:(j + 1) * P], acc_now[:, j * P:j * P + r], ident[:, :])
                last.then_inc(super_turned, 1)

            def chunk(c, h, last_chunk):
                pe.wait_ge(lists_stored, c + 1)
                pe.wait_ge(x_loaded[h], chunk_pair(c, h) * 16 * PARTS)
                for j, r in enumerate(rows_in(last_chunk)):
                    last = pe.transpose(turn_ps[:, j * P:j * P + r], x_in[0:r, h, j, :],
                                        ident[0:r, 0:r])
                last.then_inc(x_turned, 1)
                n = TAIL if last_chunk else WIDE
                pe.wait_ge(wt_ready, 1)
                pe.wait_ge(xt_ready, c + 1)
                if not early(c):
                    pe.wait_ge(y_ready, c - LAG + 1)
                pe.matmul(node_ps[:, 0:n], w_t[:, 0, :], x_t[:, 0:n], start=True, stop=True
                          ).then_inc(self_ready, 1)
                if not last_chunk:
                    turn_lists(c + 1, 1 - h)
                pe.wait_ge(self_added, c + 1)
                if not early(c):
                    turn_super(c - LAG, rows_in(False))

                with pe.Fori(0, IPC) as k:
                    for q in range(GPI):
                        g = c * GPC + k * GPI + q
                        pe.wait_ge(hot_ready, g + 1)
                        pe.wait_ge(window_added, g + 1)
                        for j in range(GT):
                            slot = q * GT + j
                            pe.wait_ge(gathered[slot], (c * IPC + k + 1) * 16)
                            last = pe.matmul(group_ps[q][:, SUMS], rows[:, slot, :],
                                             hot[:, q, j, :, :].rearrange("p t w -> p (t w)"),
                                             start=(j == 0), stop=(j == GT - 1))
                        last.then_inc(rows_used, 1)
                        pe.wait_ge(hot_summed, g + 1)
                        pe.wait_ge(sums_ready, g + 1)
                        for t in range(2):
                            pe.matmul(group_ps[q][:, MSGS], w_t[:, 1 + t, :], sums[:, q, t, :],
                                      start=(t == 0), stop=False)
                        for t in range(2):
                            last = pe.matmul(group_ps[q][:, MSGS], b_row[:, t * D:(t + 1) * D],
                                             hot_sum[:, q, t, :], start=False, stop=(t == 1))
                        last.then_inc(msgs_ready, 1)

            over_chunks(pe, chunk)

            def finish(s, count, tail):
                pe.wait_ge(y_ready, count + 1)
                turn_super(count, rows_in(tail))

            after_loop(finish)

            pe.wait_ge(worst_ready, 1)
            pe.wait_ge(y_ready, SUPERS + 1)
            pe.transpose(node_ps[0:1, 0:P], worst[:, :], ident[:, :]).then_inc(worst_turned, 1)

            pe.wait_ge(flag_ready, 1)
            general = pe.value_load(flag[0:1, 0:1], min_val=0, max_val=1)
            with pe.If(general > 0):
                with pe.Fori(0, TILES) as t:
                    pe.wait_ge(late_gathered, (t + 1) * 16)
                    pe.transpose(turn_ps[:, 0:P], late_x[:, :], ident[:, :]).then_inc(late_turned, 1)
                    pe.wait_ge(late_xt_ready, t + 1)
                    pe.matmul(group_ps[0][:, 0:2 * D], late_xt[:, :],
                              w_t[:, 1:3, :].rearrange("p k d -> p (k d)"), start=True, stop=True
                              ).then_inc(late_both_ready, 1)
                    with pe.Fori(0, WINDOWS) as w:
                        pe.wait_ge(late_hot_ready, t * WINDOWS + w + 1)
                        pe.matmul(node_ps[:, :], late_msg[:, :], late_hot[:, :], start=True, stop=True
                                  ).then_inc(late_summed, 1)

                pe.wait_ge(late_added, TILES * WINDOWS)
                again(pe, finish)

        @block.scalar
        def _(act):
            def store_sources(c):
                act.wait_ge(sources_turned, c + 1)
                act.activation(src_all[:, bass.ds(c * CH, CH)], turn_ps[:, 0:CH], ACT.Copy
                               ).then_inc(sources_stored, 1)

            def store_keys(c):
                act.wait_ge(lists_turned, c + 1)
                act.activation(key_all[:, bass.ds(c * CH, CH)], turn_ps[:, P:P + CH], ACT.Copy
                               ).then_inc(lists_stored, 1)

            def stage(g, q):
                act.activation(src_now[:, q * GT:(q + 1) * GT], src_all[:, bass.ds(g * GT, GT)], ACT.Copy
                               ).then_inc(staged, 1)

            store_sources(0)
            act.wait_ge(sources_stored, 1)
            for q in range(GPI):
                stage(q, q)
            store_keys(0)
            act.wait_ge(weights_turned, 1)
            act.activation(w_t[:, :, :].rearrange("p k d -> p (k d)"), node_ps[:, 0:3 * D], ACT.Copy
                           ).then_inc(wt_ready, 1)

            act.sem_inc(out_ready, 1)

            def copy_super(s, count, tail):
                n = TAIL if tail else WIDE
                act.wait_ge(super_turned, count + 1)
                act.activation(acc_now[:, 0:n], acc[:, bass.ds(s * WIDE, n)], ACT.Copy
                               ).then_inc(super_copied, 1)

            def normalise(s, count, tail):
                k = len(rows_in(tail))
                act.wait_ge(mv_ready, count + 1)
                act.activation(std[:, 0:k], mv[:, 0:k, 1], ACT.Sqrt, bias=eps_t[:, 0:1]).then_inc(std_ready, 1)
                act.wait_ge(scales_ready, count + 1)
                act.wait_ge(out_free, count + 1)
                for j, r in enumerate(rows_in(tail)):
                    last = act.activation(out_sb[0:r, j, :], y_sb[0:r, j, :], ACT.Identity,
                                          bias=shift[0:r, j:j + 1], scale=rstd[0:r, j:j + 1])
                last.then_inc(out_ready, 1)

            def chunk(c, h, last_chunk):
                n = TAIL if last_chunk else WIDE
                act.wait_ge(x_turned, c + 1)
                if not (isinstance(c, int) and c == 0):
                    act.wait_ge(self_ready, c)
                act.activation(x_t[:, 0:n], turn_ps[:, 0:n], ACT.Copy).then_inc(xt_ready, 1)
                if not last_chunk:
                    store_sources(c + 1)
                    store_keys(c + 1)
                if not early(c):
                    act.wait_ge(window_added, c * GPC + GPI)
                    copy_super(c - LAG, c - LAG, False)
                    normalise(c - LAG, c - LAG, False)
                if not last_chunk:
                    act.wait_ge(lists_stored, c + 2)
                with act.Fori(0, IPC) as k:
                    for q in range(GPI):
                        g = c * GPC + k * GPI + q
                        act.wait_ge(rows_used, g + 1 + GPI)
                        act.activation(sums[:, q, :, :].rearrange("p t w -> p (t w)"), group_ps[q][:, SUMS],
                                       ACT.Copy).then_inc(sums_ready, 1)
                        stage(g + GPI, q)

            act.wait_ge(pads_ready, 1)
            over_chunks(act, chunk)

            def finish(s, count, tail):
                copy_super(s, count, tail)
                normalise(s, count, tail)

            act.wait_ge(window_added, GROUPS + GPI)
            after_loop(finish)

            act.wait_ge(flag_ready, 1)
            general = act.value_load(flag[0:1, 0:1], min_val=0, max_val=1)
            with act.If(general > 0):
                with act.Fori(0, TILES) as t:
                    act.wait_ge(late_turned, t + 1)
                    act.activation(late_xt[:, :], turn_ps[:, 0:P], ACT.Copy).then_inc(late_xt_ready, 1)
                act.wait_ge(late_added, TILES * WINDOWS)
                again(act, finish)

        @block.vector
        def _(dve):
            dve.sem_inc(window_added, GPI)
            dve.sem_inc(y_ready, 1)
            dve.memset(eps_t[:, :], EPS)
            dve.memset(minus_one[:, :], -1.0)
            dve.memset(mv[:, :, :], 1.0)
            dve.memset(worst[:, :], -1.0)
            dve.memset(src_all[:, TILES:TILES + RING], 0.0)
            dve.memset(key_all[:, TILES:TILES + GT], -1.0)

            def take_sources(c, h):
                dve.wait_ge(sources_loaded[h], chunk_pair(c, h) * 16)
                if not (isinstance(c, int) and c < 2):
                    dve.wait_ge(lists_turned, c - 1)
                dve.tensor_copy(src_f[:, h, :], src_n[:, h, :]).then_inc(sources_ready, 1)

            take_sources(0, 0)
            dve.memset(acc[:, :], 0.0).then_inc(pads_ready, 1)

            dve.wait_ge(bases_loaded, 16 * (1 + GT))
            dve.tensor_copy(base_f[:, :], base_n[:, :]).then_inc(start_step, 1)
            dve.wait_ge(start_step, 1)

            def prepare_lists(c, h):
                dve.wait_ge(edges_loaded[h], chunk_pair(c, h) * 32)
                dve.tensor_scalar(rel_f[:, h, :], dst_n[:, h, :], base_f[:, bass.ds(c, 1)], None,
                                  ALU.subtract).then_inc(rel_ready, 1)
                dve.wait_ge(rel_ready, c + 1)
                dve.scalar_tensor_tensor(out=key_f[:, h, :], in0=typ_n[:, h, :], scalar=float(TYPE_STEP),
                                         in1=rel_f[:, h, :], op0=ALU.mult, op1=ALU.add
                                         ).then_inc(lists_ready, 1)
                dve.tensor_reduce(rel_max[:, bass.ds(c, 1)], rel_f[:, h, :], AX.X, ALU.max)
                dve.tensor_reduce(rel_min[:, bass.ds(c, 1)], rel_f[:, h, :], AX.X, ALU.min
                                  ).then_inc(worst_step, 1)

            prepare_lists(0, 0)
            dve.wait_ge(iota_ready, 3)
            dve.tensor_copy(hot_ps[:, 0:2 * WIN], hot_i[:, :, :].rearrange("p t w -> p (t w)")
                            ).then_inc(start_step, 1)
            dve.tensor_copy(iota_w[:, :], iota_i[:, :]).then_inc(start_step, 1)
            dve.wait_ge(start_step, 3)

            def make_hot(g, q):
                dve.wait_ge(msgs_ready, g + 1)
                keys = key_all[:, bass.ds(g * GT, GT)]
                dve.tensor_tensor(hot[:, q, :, :, :].rearrange("p j t w -> p j (t w)"),
                                  hot_ps[:, 0:2 * WIN].unsqueeze(1).to_broadcast([P, GT, 2 * WIN]),
                                  keys.unsqueeze(2).to_broadcast([P, GT, 2 * WIN]),
                                  ALU.is_equal).then_inc(hot_ready, 1)
                dve.wait_ge(hot_ready, g + 1)
                dve.tensor_reduce(hot_sum[:, q, :, :].rearrange("p t w -> p (t w)"),
                                  hot[:, q, :, :, :].rearrange("p j t w -> p (t w) j"),
                                  AX.X, ALU.add).then_inc(hot_summed, 1)

            def add_group(g, q):
                base = dve.value_load(bases[0:1, bass.ds(g, 1)], min_val=0, max_val=N - 1)
                dve.wait_ge(msgs_ready, g + 1 + GPI)
                dve.wait_ge(window_added, g + GPI)
                window = acc[:, bass.ds(base, WIN)]
                dve.tensor_tensor(window, group_ps[q][:, MSGS], window, ALU.add).then_inc(window_added, 1)

            def finish(s, count, tail):
                rows_of = rows_in(tail)
                k = len(rows_of)
                dve.wait_ge(super_turned, count + 2)
                dve.wait_ge(res_loaded, (count + 1) * 16 * PARTS)
                dve.wait_ge(out_ready, count + 1)
                if tail:
                    for j, r in enumerate(rows_of):
                        last = dve.scalar_tensor_tensor(out=y_sb[0:r, j, :], in0=node_ps[0:r, j * P:(j + 1) * P],
                                                        scalar=0.0, in1=x_res[0:r, j, :],
                                                        op0=ALU.max, op1=ALU.add)
                else:
                    last = dve.scalar_tensor_tensor(
                        out=y_sb[:, :, :], in0=node_ps[:, :].rearrange("p (j d) -> p j d", d=D), scalar=0.0,
                        in1=x_res[:, :, :], op0=ALU.max, op1=ALU.add)
                last.then_inc(y_ready, 1)
                dve.wait_ge(y_ready, count + 2)
                for j, r in enumerate(rows_of):
                    last = dve.bn_stats(stats[0:r, j, :], y_sb[0:r, j, :])
                last.then_inc(dve_step, 1)
                dve.wait_ge(dve_step, 2 * count + 1)
                dve.sem_inc(dve_turn, 1)
                for j, r in enumerate(rows_of):
                    last = dve.bn_aggr(mv[0:r, j, :], stats[0:r, j, :])
                last.then_inc(mv_ready, 1)
                dve.wait_ge(mv_ready, count + 1)
                dve.wait_ge(std_ready, count + 1)
                dve.reciprocal(rstd[:, 0:k], std[:, 0:k]).then_inc(dve_step, 1)
                dve.wait_ge(dve_step, 2 * count + 2)
                dve.scalar_tensor_tensor(out=shift[:, 0:k], in0=mv[:, 0:k, 0], scalar=-1.0, in1=rstd[:, 0:k],
                                         op0=ALU.mult, op1=ALU.mult).then_inc(scales_ready, 1)

            def chunk(c, h, last_chunk):
                if not last_chunk:
                    take_sources(c + 1, 1 - h)
                    prepare_lists(c + 1, 1 - h)
                n = TAIL if last_chunk else WIDE
                dve.wait_ge(self_ready, c + 1)
                dve.wait_ge(window_added, c * GPC + GPI)
                nodes = acc[:, bass.ds(c * WIDE, n)]
                dve.scalar_tensor_tensor(out=nodes, in0=node_ps[:, 0:n], scalar=b_col[:, 0:1], in1=nodes,
                                         op0=ALU.add, op1=ALU.add).then_inc(self_added, 1)
                if not early(c):
                    finish(c - LAG, c - LAG, False)
                if not last_chunk:
                    dve.wait_ge(lists_stored, c + 2)
                dve.wait_ge(self_added, c + 1)
                dve.sem_inc(dve_turn, 1)
                with dve.Fori(0, IPC) as k:
                    for q in range(GPI):
                        g = c * GPC + k * GPI + q
                        make_hot(g + 1, (q + 1) % GPI)
                        add_group(g, q)

            dve.wait_ge(pads_ready, 1)
            dve.wait_ge(weights_loaded, 16 * 6)
            dve.wait_ge(lists_stored, 1)
            make_hot(0, 0)
            over_chunks(dve, chunk)

            dve.wait_ge(worst_step, CHUNKS)
            dve.tensor_single_scalar(out_of[:, 0, :], rel_max[:, :], float(1 - WIN), ALU.add)
            dve.tensor_single_scalar(out_of[:, 1, :], rel_min[:, :], -1.0, ALU.mult)
            dve.tensor_tensor(out_of[:, 3, :], rel_min[:, :], base_f[:, :], ALU.add).then_inc(worst_step, 1)
            dve.wait_ge(worst_step, CHUNKS + 1)
            dve.tensor_tensor(out_of[:, 2, :], floor_i[:, :], out_of[:, 3, :], ALU.subtract
                              ).then_inc(worst_step, 1)
            dve.wait_ge(worst_step, CHUNKS + 2)
            dve.tensor_reduce(worst[0:CH, :], out_of[:, 0:3, :].rearrange("p k c -> p (k c)"), AX.X, ALU.max
                              ).then_inc(worst_ready, 1)

            after_loop(finish)

            dve.wait_ge(worst_turned, 1)
            dve.tensor_reduce(viol[:, :], node_ps[0:1, 0:P], AX.X, ALU.max).then_inc(worst_step, 1)
            dve.wait_ge(worst_step, CHUNKS + 3)
            dve.tensor_single_scalar(flag[:, :], viol[:, :], 0.0, ALU.is_gt).then_inc(flag_ready, 1)
            dve.wait_ge(flag_ready, 1)

            general = dve.value_load(flag[0:1, 0:1], min_val=0, max_val=1)
            with dve.If(general > 0):
                dve.sem_inc(late_tile_done, 1)
                STEPS = 6 + WINDOWS
                with dve.Fori(0, TILES) as t:
                    def step(k, ins):
                        ins.then_inc(late_step, 1)
                        dve.wait_ge(late_step, t * STEPS + k)

                    dve.tensor_copy(late_src[:, :], src_all[:, bass.ds(t, 1)]).then_inc(late_index, 1)
                    dve.wait_ge(late_loaded, (t + 1) * 32)
                    step(1, dve.tensor_copy(late[:, 0:1], late_typ[:, :]))
                    dve.scalar_tensor_tensor(out=late[:, 1:2], in0=late[:, 0:1], scalar=float(-TYPE_STEP),
                                             in1=key_all[:, bass.ds(t, 1)], op0=ALU.mult, op1=ALU.add)
                    dve.tensor_scalar(late[:, 7:8], late[:, 0:1], -1.0, 1.0, ALU.mult, ALU.add)
                    step(2, dve.tensor_single_scalar(late[:, 6:7], late_dst[:, :], 1.0, ALU.add))
                    dve.tensor_single_scalar(late[:, 2:3], late[:, 1:2], 0.0, ALU.is_ge)
                    step(3, dve.tensor_single_scalar(late[:, 3:4], late[:, 1:2], float(WIN), ALU.is_lt))
                    step(4, dve.tensor_tensor(late[:, 4:5], late[:, 2:3], late[:, 3:4], ALU.mult))
                    step(5, dve.tensor_scalar(late[:, 5:6], late[:, 4:5], -1.0, 1.0, ALU.mult, ALU.add))
                    step(6, dve.scalar_tensor_tensor(out=late_key[:, :], in0=late[:, 5:6],
                                                     scalar=late[:, 6:7], in1=minus_one[:, :],
                                                     op0=ALU.mult, op1=ALU.add))
                    dve.wait_ge(late_both_ready, t + 1)
                    dve.tensor_tensor(late_both[:, :], group_ps[0][:, 0:2 * D], b_row[:, :], ALU.add
                                      ).then_inc(late_msg_step, 1)
                    dve.wait_ge(late_msg_step, t * 3 + 1)
                    dve.tensor_scalar(late_part[:, :], late_both[:, D:2 * D], late[:, 0:1], None, ALU.mult
                                      ).then_inc(late_msg_step, 1)
                    dve.wait_ge(late_msg_step, t * 3 + 2)
                    dve.scalar_tensor_tensor(out=late_msg[:, :], in0=late_both[:, 0:D], scalar=late[:, 7:8],
                                             in1=late_part[:, :], op0=ALU.mult, op1=ALU.add
                                             ).then_inc(late_msg_step, 1)
                    dve.wait_ge(late_msg_step, t * 3 + 3)
                    dve.sem_inc(dve_turn, 1)
                    with dve.Fori(0, WINDOWS) as w:
                        dve.tensor_scalar(late_hot[:, :], iota_w[:, :], late_key[:, 0:1], None, ALU.is_equal
                                          ).then_inc(late_hot_ready, 1)
                        dve.wait_ge(late_hot_ready, t * WINDOWS + w + 1)
                        dve.tensor_single_scalar(late_key[:, :], late_key[:, :], float(-WIDE), ALU.add
                                                 ).then_inc(late_step, 1)
                        dve.wait_ge(late_summed, t * WINDOWS + w + 1)
                        nodes = acc[:, bass.ds(w * WIDE, WIDE)]
                        dve.tensor_tensor(nodes, node_ps[:, :], nodes, ALU.add).then_inc(late_added, 1)
                        dve.wait_ge(late_added, t * WINDOWS + w + 1)
                        dve.wait_ge(late_step, t * STEPS + 6 + w + 1)
                    dve.sem_inc(late_tile_done, 1)
                again(dve, finish)


_INS = ["x", "src", "dst", "edge_type_2", "L0_gnn_W_data", "L0_gnn_b_data", "L0_gnn_W_control",
        "L0_gnn_b_control", "L0_gnn_W_self", "L0_gnn_b_self"]


def kernel(**inputs):
    import concourse.bacc as bacc
    from concourse.bass_utils import run_bass_kernel_spmd

    nc = bacc.Bacc("TRN2", target_bir_lowering=False, num_devices=1)
    arrays, args = {}, []
    for name in _INS:
        a = np.ascontiguousarray(inputs[name])
        arrays[f"in_{name}"] = a
        args.append(nc.dram_tensor(f"in_{name}", a.shape, mybir.dt.from_np(a.dtype), kind="ExternalInput").ap())
    out = nc.dram_tensor("out", arrays["in_x"].shape, F32, kind="ExternalOutput").ap()
    gnn_resnorm(nc, *args, out)
    r = run_bass_kernel_spmd(nc, [arrays], core_ids=[0])
    return r.results[0]["out"]
```
